# Optimizing a Trainium2 kernel written in Bass

```python
import numpy as np
import jax
import jax.numpy as jnp

def _softmax(x, axis=-1):
    return jax.nn.softmax(x, axis=axis)

def _gelu(x):
    return jax.nn.gelu(x, approximate=True)

def _silu(x):
    return jax.nn.silu(x)

def _sigmoid(x):
    return jax.nn.sigmoid(x)

def _layernorm(x, axis=-1, eps=1e-05):
    m = jnp.mean(x, axis=axis, keepdims=True)
    v = jnp.var(x, axis=axis, keepdims=True)
    return (x - m) / jnp.sqrt(v + eps)

def _scatter_add(tgt, idx, src, axis=0):
    return tgt.at[idx].add(src)

def _segment_sum(src, seg, n):
    return jax.ops.segment_sum(src, seg, n)
kernel_name = 'mk_adj_resnorm_d1_adj_r2_db125b'

def setup_inputs(seed: int=0):
    np.random.seed(seed)
    _w = jnp.asarray

    def _rec_inputs():
        import jax
        import jax.numpy as jnp
        _gk = jax.random.key(seed)
        x = -0.0002928 + 1 * jax.random.normal(jax.random.fold_in(_gk, 1), (4096, 256), jnp.float32)
        _a = jax.random.bernoulli(jax.random.fold_in(_gk, 2), 0.000488281, (4096, 4096))
        _af = _a.astype(jnp.float32)
        adj = _af
        return (x, adj)
    x, adj = _rec_inputs()

    def _L0_gnn_setup():
        import jax, jax.numpy as jnp
        import numpy as np
        N = 4096
        D = 256
        L = 2
        NEG_SLOPE = 0.01

        def _gat_layer(x, W, adj):
            proj = x @ W
            Wh, Ws = jnp.split(proj, 2, axis=-1)
            scores = Wh @ Ws.T
            a = jax.nn.softmax(scores, axis=-1) * adj
            out = a @ Wh
            out = out + x
            return jax.nn.leaky_relu(out, NEG_SLOPE)
        key = jax.random.key(seed)
        k1, k2, k3 = jax.random.split(key, 3)
        inputs = jax.random.normal(k1, (N, D), dtype=jnp.float32)
        adj = jax.random.randint(k2, (N, N), 0, 2).astype(jnp.float32)
        W_stack = jax.random.normal(k3, (L, D, 2 * D), dtype=jnp.float32) * (1.0 / np.sqrt(D))
        return {'inputs': inputs, 'adj': adj, 'W_stack': W_stack}
    _L0_gnn_all = _L0_gnn_setup()
    _L0_gnn_in = {k: v for k, v in _L0_gnn_all.items() if k in ('W_stack',)}
    del _L0_gnn_all
    return {'x': x, 'adj': adj, 'L0_gnn_W_stack': _L0_gnn_in['W_stack']}

def reference(x, adj, L0_gnn_W_stack):
    import jax
    import jax.numpy as jnp

    def _L0_gnn_ref(inputs, adj, W_stack):
        import jax, jax.numpy as jnp
        import numpy as np
        N = 4096
        D = 256
        L = 2
        NEG_SLOPE = 0.01

        def _gat_layer(x, W, adj):
            proj = x @ W
            Wh, Ws = jnp.split(proj, 2, axis=-1)
            scores = Wh @ Ws.T
            a = jax.nn.softmax(scores, axis=-1) * adj
            out = a @ Wh
            out = out + x
            return jax.nn.leaky_relu(out, NEG_SLOPE)
        x = inputs
        for l in range(W_stack.shape[0]):
            x = _gat_layer(x, W_stack[l], adj)
        return x
    x = _layernorm(x + _L0_gnn_ref(x, adj, L0_gnn_W_stack), axis=-1)
    return x

_drawn_inputs = setup_inputs


def setup_inputs(seed=0):
    import zlib

    import numpy as np

    out = dict(_drawn_inputs(seed))
    spreads = {}
    factors = {'adj': 5.753, 'L0_gnn_W_stack': 6.469}
    for name, (base, spread) in spreads.items():
        noise = np.random.default_rng([zlib.crc32(name.encode()), seed]).standard_normal(out[name].shape)
        drawn = base * np.exp(spread * noise) if base else spread * noise
        out[name] = jnp.asarray(drawn.astype(out[name].dtype))
    for name, factor in factors.items():
        out[name] = (out[name] * factor).astype(out[name].dtype)
    return out
```

```python
from contextlib import ExitStack

import concourse.bass as bass
from concourse import mybir

F32 = mybir.dt.float32
F32R = mybir.dt.float32r
ALU = mybir.AluOpType
ACT = mybir.ActivationFunctionType
AXIS_X = mybir.AxisListType.X

P = 128
LAYERS = 2
SLOPE = 0.01
EPS = 1e-5


def gat_layernorm(nc, x, adj, w, out):
    N, D = x.shape
    KT = D // P
    TILES = N // P
    CHUNK = 512
    CHUNKS = N // CHUNK
    BLOCKS = CHUNK // P
    STEPS = TILES * CHUNKS
    RING = 2 * CHUNKS
    LAG_WEIGHT = CHUNKS + 1
    LAG_TRANSPOSE = CHUNKS + 2
    LAG_PRODUCT = CHUNKS + 3
    LAG_ROWS = 2 * CHUNKS + 3
    LAG_NORM = LAG_ROWS + 1
    SCORE_BANKS = 4
    ADJ_SLOTS = 4
    PIECE = 2 * CHUNK
    PIECES = N // PIECE
    GROUP = 2 * P
    GROUPS = N // GROUP

    adj_pieces = adj.rearrange("(t p) (q c) -> t q p c", p=P, c=PIECE)
    x1 = nc.dram_tensor("x1_scratch", [N, D], F32).ap()
    wht_tiles = nc.dram_tensor("wht_scratch", [TILES, P, 2 * KT * P], F32).ap()
    wht_groups = wht_tiles.rearrange("(g t) p e -> g p t e", t=2)
    layer_in = [x, x1]
    in_tiles = [a.rearrange("(t p) d -> t p d", p=P) for a in layer_in]
    in_groups = [a.rearrange("(g t p) d -> g p t d", p=P, t=2) for a in layer_in]
    out_tiles = [in_tiles[1], out.rearrange("(t p) d -> t p d", p=P)]

    ctx = ExitStack()
    with ctx:
        def sb(name, shape, dt=F32):
            return ctx.enter_context(nc.sbuf_tensor(name, shape, dt))

        def sem(name):
            return ctx.enter_context(nc.semaphore(name))

        def sem_pair(name):
            return [sem(f"{name}{p}") for p in range(2)]

        ws_t = sb("ws_t", [P, 2, KT, N], F32R)
        wh = sb("wh", [P, TILES, 2, D], F32R)
        wh_t = sb("wh_t", [P, 2, 2, 2, KT, P], F32R)
        w_part = sb("w_part", [P, 2, KT, 2 * D], F32R)
        moving_hi = sb("moving_hi", [P, 2, CHUNK], F32R)
        moving_lo = sb("moving_lo", [P, 2, CHUNK], F32R)
        ring = sb("ring", [P, RING, CHUNK])
        load = sb("load", [P, ADJ_SLOTS, PIECE])
        rows = sb("rows", [P, 2, D])
        first_rows = sb("first_rows", [P, 2, D])
        ident = sb("ident", [P, P])
        neg_max = sb("neg_max", [P, RING])
        chunk_sum = sb("chunk_sum", [P, RING])
        row_neg_max = sb("row_neg_max", [P, 2])
        factor = sb("factor", [P, RING])
        scaled_sum = sb("scaled_sum", [P, RING])
        row_sum = sb("row_sum", [P, 2])
        row_inv = sb("row_inv", [P, 2])
        weight = sb("weight", [P, RING])
        stats = sb("stats", [P, 6])
        moments = sb("moments", [P, 2])
        var_eps = sb("var_eps", [P, 1])
        minus_half = sb("minus_half", [P, 1])
        inv_std = sb("inv_std", [P, 1])

        psum = ctx.enter_context(nc.psum_tensor("banks", [P, 8, CHUNK], F32))
        XT_BANK, WST_BANK, WHT_BANK, WH_BANK = 0, 2, 4, 6
        SCORE_BANK, AT_BANK, ACC_BANK = 0, 4, 6

        pool_step, ident_done = sem("pool_step"), sem("ident_done")
        w_loaded, w_hi, w_lo = sem("w_loaded"), sem("w_hi"), sem("w_lo")
        x_loaded = sem_pair("x_loaded")
        xt_done, xt_hi, xt_lo = sem("xt_done"), sem("xt_hi"), sem("xt_lo")
        wst_done, wst_hi, wst_lo = sem("wst_done"), sem("wst_hi"), sem("wst_lo")
        wht_done, wht_hi, wht_lo = sem("wht_done"), sem("wht_hi"), sem("wht_lo")
        wh_hi_done, wh_lo_done = sem("wh_hi_done"), sem("wh_lo_done")
        wh_hi_copied = sem("wh_hi_copied")
        wht_stored, wht_loaded = sem_pair("wht_stored"), sem_pair("wht_loaded")
        adj_loaded = [sem(f"adj_loaded{s}") for s in range(ADJ_SLOTS)]
        scores_done, max_done, exp_done = sem("scores_done"), sem("max_done"), sem("exp_done")
        row_max_done, factor_done = sem("row_max_done"), sem("factor_done")
        stat_step = sem("stat_step")
        a_done, at_done, at_hi, at_lo = sem("a_done"), sem("at_done"), sem("at_hi"), sem("at_lo")
        product_done = sem("product_done")
        acc_free = sem("acc_free")
        row_step = sem("row_step")
        rows_loaded, first_loaded = sem_pair("rows_loaded"), sem_pair("first_loaded")
        var_done, inv_std_done = sem("var_done"), sem("inv_std_done")
        rows_done, rows_stored = sem("rows_done"), sem_pair("rows_stored")

        PAIRS = TILES // 2
        GROUP_PAIRS = GROUPS // 2
        ACC_FREE = GROUPS + TILES
        STAT_STEPS = 4
        ROW_STEPS = [1, 5]

        def as_f32(ap):
            return ap.bitcast(F32)

        def peeled(pair):
            return isinstance(pair, int)

        def each_group(eng, group):
            for p in range(2):
                group(0, p)
            with eng.Fori(1, GROUP_PAIRS - 1) as pair:
                for p in range(2):
                    group(pair, p)
            for p in range(2):
                group(GROUP_PAIRS - 1, p)

        def each_step(eng, step, lag):
            for k in range(RING):
                step(0, k)
            with eng.Fori(1, PAIRS) as pair:
                for k in range(RING):
                    step(pair, k)
            for k in range(lag):
                step(PAIRS, k)

        def in_stage(pair, k, lag):
            return not peeled(pair) or 0 <= RING * pair + k - lag < STEPS

        def chunk_of(pair, k, lag):
            t = (k - lag) // CHUNKS
            return RING * pair + (k - lag), (k - lag) % RING, 2 * pair + t, t % 2, pair + t // 2

        block = ctx.enter_context(nc.Block())

        @block.sync
        def _(sp):
            for layer in range(LAYERS):
                groups0, steps0 = layer * GROUPS, layer * STEPS

                def load_x(g, p):
                    if layer:
                        sp.wait_ge(rows_stored[0], 16 * (g + 1))
                        sp.wait_ge(rows_stored[1], 16 * (g + 1))
                    sp.dma_start(load[:, p, 0:2 * D].rearrange("p (t d) -> p t d", t=2),
                                 in_groups[layer][g]).then_inc(x_loaded[p], 16)

                if layer:
                    sp.wait_ge(a_done, steps0 - 2)
                sp.dma_start(load[:, 2, :].rearrange("p (k e) -> p k e", k=KT),
                             w[layer].rearrange("(k p) e -> p k e", p=P)).then_inc(w_loaded, 16)
                load_x(0, 0)
                load_x(1, 1)
                with sp.Fori(1, GROUP_PAIRS) as pair:
                    for p in range(2):
                        sp.wait_ge(xt_done, groups0 + 2 * pair + p - 1)
                        load_x(2 * pair + p, p)

                def load_wh_t(pair, p):
                    sp.dma_start(as_f32(wh_t[:, p, 0]).rearrange("p a k n -> p (a k n)"),
                                 wht_tiles[2 * pair + p]).then_inc(wht_loaded[p], 16)

                def load_adj(tile, q):
                    sp.dma_start(load[:, q, :], adj_pieces[tile, q]).then_inc(adj_loaded[q], 16)

                for p in range(2):
                    sp.wait_ge(wht_stored[p], 16 * GROUP_PAIRS * (layer + 1))
                sp.wait_ge(wh_lo_done, groups0 + GROUPS)
                load_wh_t(0, 0)
                load_wh_t(0, 1)
                sp.wait_ge(w_lo, layer + 1)
                sp.wait_ge(xt_done, groups0 + GROUPS)
                if layer:
                    sp.wait_ge(a_done, steps0)
                for q in range(PIECES):
                    load_adj(0, q)
                with sp.Fori(1, PAIRS) as pair:
                    for p in range(2):
                        sp.wait_ge(scores_done, steps0 + CHUNKS * (2 * pair + p - 1))
                        load_wh_t(pair, p)
                        for q in range(PIECES):
                            sp.wait_ge(a_done, steps0 + CHUNKS * (2 * pair + p - 2) + 2 * (q + 1))
                            load_adj(2 * pair + p - 1, q)
                for q in range(PIECES):
                    sp.wait_ge(a_done, steps0 + CHUNKS * (TILES - 2) + 2 * (q + 1))
                    load_adj(TILES - 1, q)

        @block.tensor
        def _(pe):
            def three_products(out_ap, operands):
                for j, (s_hi, s_lo, m_hi, m_lo) in enumerate(operands):
                    nc.tensor.matmul(out_ap, s_hi, m_hi, start=j == 0, stop=False)
                    nc.tensor.matmul(out_ap, s_hi, m_lo, start=False, stop=False)
                    last = nc.tensor.matmul(out_ap, s_lo, m_hi, start=False, stop=j == len(operands) - 1)
                return last

            pe.wait_ge(ident_done, 1)
            for layer in range(LAYERS):
                groups0, steps0 = layer * GROUPS, layer * STEPS

                def transpose_x(g, p, pair):
                    pe.wait_ge(x_loaded[p], 16 * (layer * GROUP_PAIRS + pair + 1))
                    for t in range(2):
                        for kt in range(KT):
                            last = nc.tensor.transpose(
                                psum[:, XT_BANK + p, kt * GROUP + t * P:kt * GROUP + (t + 1) * P],
                                load[:, p, t * D + kt * P:t * D + (kt + 1) * P], ident[:])
                    last.then_inc(xt_done, 1)

                def project(out_bank, p, column):
                    for dt in range(KT):
                        cols = slice(column + dt * P, column + (dt + 1) * P)
                        rows_of = [slice(kt * GROUP, (kt + 1) * GROUP) for kt in range(KT)]
                        last = three_products(
                            psum[:, out_bank, dt * GROUP:(dt + 1) * GROUP],
                            [(w_part[:, 0, kt, cols], w_part[:, 1, kt, cols],
                              moving_hi[:, p, rows_of[kt]], moving_lo[:, p, rows_of[kt]]) for kt in range(KT)])
                    return last

                def transpose_wh(g, p, first):
                    pe.wait_ge(wht_lo, groups0 + g + 1)
                    if not first:
                        pe.wait_ge(wh_hi_copied, groups0 + g)
                        pe.wait_ge(acc_free, layer * ACC_FREE + g)
                    for part, done in ((0, wh_hi_done), (1, wh_lo_done)):
                        for t in range(2):
                            for dt in range(KT):
                                last = nc.tensor.transpose(
                                    psum[:, WH_BANK + part, t * D + dt * P:t * D + (dt + 1) * P],
                                    as_f32(wh_t[:, p, t, part, dt]), ident[:])
                        last.then_inc(done, 1)

                def group(pair, p):
                    g = 2 * pair + p
                    first, second = peeled(pair) and g == 0, peeled(pair) and g == 1
                    if not (peeled(pair) and g == GROUPS - 1):
                        if not first:
                            pe.wait_ge(xt_lo, groups0 + g)
                        transpose_x(g + 1, 1 - p, pair + p)
                    pe.wait_ge(xt_lo, groups0 + g + 1)
                    if not (first or second):
                        pe.wait_ge(wst_lo, groups0 + g - 1)
                    project(WST_BANK + p, p, D).then_inc(wst_done, 1)
                    if not first:
                        transpose_wh(g - 1, 1 - p, second)
                    project(WHT_BANK + p, p, 0).then_inc(wht_done, 1)

                if layer:
                    pe.wait_ge(exp_done, steps0)
                transpose_x(0, 0, 0)
                pe.wait_ge(w_lo, layer + 1)
                if layer:
                    pe.wait_ge(at_lo, steps0)
                    pe.wait_ge(acc_free, layer * ACC_FREE)
                each_group(pe, group)
                transpose_wh(GROUPS - 1, 1, False)

                pe.wait_ge(wst_lo, groups0 + GROUPS)
                pe.wait_ge(wh_hi_copied, groups0 + GROUPS)

                def scores(pair, k):
                    n, slot, _, p, before = chunk_of(pair, k, 0)
                    if k % CHUNKS == 0:
                        pe.wait_ge(wht_loaded[p], 16 * (layer * PAIRS + before + 1))
                    if not peeled(pair) or n >= SCORE_BANKS:
                        pe.wait_ge(exp_done, steps0 + n - SCORE_BANKS + 1)
                    cols = slice(k % CHUNKS * CHUNK, (k % CHUNKS + 1) * CHUNK)
                    three_products(psum[:, SCORE_BANK + k % SCORE_BANKS, :],
                                   [(wh_t[:, p, 0, 0, kt], wh_t[:, p, 0, 1, kt],
                                     ws_t[:, 0, kt, cols], ws_t[:, 1, kt, cols]) for kt in range(KT)]
                                   ).then_inc(scores_done, 1)

                def transpose_a(pair, k):
                    m, slot, _, _, _ = chunk_of(pair, k, LAG_TRANSPOSE)
                    pe.wait_ge(a_done, steps0 + m + 1)
                    if not peeled(pair) or m >= 2:
                        pe.wait_ge(at_lo, steps0 + m - 1)
                    for b in range(BLOCKS):
                        last = nc.tensor.transpose(psum[:, AT_BANK + slot % 2, b * P:(b + 1) * P],
                                                   ring[:, slot, b * P:(b + 1) * P], ident[:])
                    last.then_inc(at_done, 1)

                def product(pair, k):
                    m, slot, tile, p, _ = chunk_of(pair, k, LAG_PRODUCT)
                    bank, c = ACC_BANK + p, slot % CHUNKS
                    pe.wait_ge(at_lo, steps0 + m + 1)
                    if c == 0:
                        free = 0 if peeled(pair) and tile < 2 else tile - 1
                        pe.wait_ge(acc_free, layer * ACC_FREE + GROUPS + free)
                    for b in range(BLOCKS):
                        j, of = c * BLOCKS + b, slice(b * P, (b + 1) * P)
                        start, stop = j == 0, j == TILES - 1
                        nc.tensor.matmul(psum[:, bank, :], moving_hi[:, slot % 2, of],
                                         wh[:, j].rearrange("p a d -> p (a d)"),
                                         start=start, stop=stop, skip_group_check=True)
                        last = nc.tensor.matmul(psum[:, bank, 0:D], moving_lo[:, slot % 2, of], wh[:, j, 0],
                                                start=False, stop=stop, skip_group_check=True)
                    last.then_inc(product_done, 1)

                def step(pair, k):
                    if in_stage(pair, k, 0):
                        scores(pair, k)
                    if in_stage(pair, k, LAG_TRANSPOSE):
                        transpose_a(pair, k)
                    if in_stage(pair, k, LAG_PRODUCT):
                        product(pair, k)

                each_step(pe, step, LAG_PRODUCT)

        @block.scalar
        def _(act):
            for layer in range(LAYERS):
                groups0, steps0, tiles0 = layer * GROUPS, layer * STEPS, layer * TILES

                act.wait_ge(w_loaded, 16 * (layer + 1))
                nc.scalar.activation(w_part[:, 0].rearrange("p k e -> p (k e)"), load[:, 2, :],
                                     ACT.Copy).then_inc(w_hi, 1)

                def split_x(g, p, free):
                    act.wait_ge(xt_done, groups0 + g + 1)
                    if not free:
                        act.wait_ge(wht_done, groups0 + g - 1)
                    nc.scalar.activation(moving_hi[:, p, :], psum[:, XT_BANK + p, :], ACT.Copy).then_inc(xt_hi, 1)

                def copy_wh(pair, p):
                    g = 2 * pair + p
                    act.wait_ge(wh_hi_done, groups0 + g + 1)
                    nc.scalar.activation(wh[:, bass.ds(2 * g, 2), 0, :],
                                         psum[:, WH_BANK, :].rearrange("p (t d) -> p t d", t=2),
                                         ACT.Copy).then_inc(wh_hi_copied, 1)

                def group(pair, p):
                    g = 2 * pair + p
                    if not (peeled(pair) and g == GROUPS - 1):
                        split_x(g + 1, 1 - p, peeled(pair) and g == 0)
                    act.wait_ge(wst_done, groups0 + g + 1)
                    nc.scalar.activation(ws_t[:, 0, :, bass.ds(GROUP * g, GROUP)],
                                         psum[:, WST_BANK + p, :].rearrange("p (k n) -> p k n", k=KT),
                                         ACT.Copy).then_inc(wst_hi, 1)
                    if not (peeled(pair) and g == 0):
                        copy_wh(pair + p - 1, 1 - p)
                    act.wait_ge(wht_done, groups0 + g + 1)
                    if not (peeled(pair) and pair == 0):
                        act.wait_ge(wht_stored[p], 16 * (layer * GROUP_PAIRS + pair))
                        act.wait_ge(wh_lo_done, groups0 + g - 1)
                    for t in range(2):
                        by_tile = psum[:, WHT_BANK + p, :].rearrange("p (k t n) -> p k t n", k=KT, t=2)
                        last = nc.scalar.activation(wh_t[:, p, t, 0], by_tile[:, :, t], ACT.Copy)
                    last.then_inc(wht_hi, 1)

                split_x(0, 0, True)
                each_group(act, group)
                copy_wh(GROUP_PAIRS - 1, 1)

                def exponentials(pair, k):
                    n, slot, tile, p, _ = chunk_of(pair, k, 0)
                    act.wait_ge(max_done, steps0 + n + 1)
                    if not peeled(pair):
                        act.wait_ge(at_done, steps0 + n - RING + 1)
                    nc.scalar.activation(ring[:, slot, :], psum[:, SCORE_BANK + k % SCORE_BANKS, :], ACT.Exp,
                                         bias=neg_max[:, slot:slot + 1],
                                         accum_out=chunk_sum[:, slot:slot + 1]).then_inc(exp_done, 1)
                    if k % CHUNKS == CHUNKS - 1:
                        of = slice(p * CHUNKS, (p + 1) * CHUNKS)
                        act.wait_ge(row_max_done, tiles0 + tile + 1)
                        nc.scalar.activation(factor[:, of], neg_max[:, of], ACT.Exp,
                                             bias=row_neg_max[:, p:p + 1], scale=-1.0).then_inc(factor_done, 1)

                def split_a(pair, k):
                    m, slot, _, _, _ = chunk_of(pair, k, LAG_TRANSPOSE)
                    act.wait_ge(at_done, steps0 + m + 1)
                    if not peeled(pair) or m >= 2:
                        act.wait_ge(product_done, steps0 + m - 1)
                    nc.scalar.activation(moving_hi[:, slot % 2, :], psum[:, AT_BANK + slot % 2, :],
                                         ACT.Copy).then_inc(at_hi, 1)

                def step(pair, k):
                    if in_stage(pair, k, 0):
                        exponentials(pair, k)
                    if in_stage(pair, k, LAG_TRANSPOSE):
                        split_a(pair, k)

                each_step(act, step, LAG_TRANSPOSE)

        @block.vector
        def _(dve):
            def low(out_ap, value, hi):
                return nc.vector.tensor_tensor(out_ap, value, as_f32(hi), ALU.subtract)

            for layer in range(LAYERS):
                groups0, steps0, tiles0 = layer * GROUPS, layer * STEPS, layer * TILES
                last_layer = layer == LAYERS - 1

                dve.wait_ge(w_hi, layer + 1)
                low(w_part[:, 1].rearrange("p k e -> p (k e)"), load[:, 2, :],
                    w_part[:, 0].rearrange("p k e -> p (k e)")).then_inc(w_lo, 1)

                def split_x(g, p):
                    dve.wait_ge(xt_hi, groups0 + g + 1)
                    low(moving_lo[:, p, :], psum[:, XT_BANK + p, :], moving_hi[:, p, :]).then_inc(xt_lo, 1)

                def copy_wh(pair, p):
                    g = 2 * pair + p
                    dve.wait_ge(wh_lo_done, groups0 + g + 1)
                    nc.vector.tensor_copy(wh[:, bass.ds(2 * g, 2), 1, :],
                                          psum[:, WH_BANK + 1, :].rearrange("p (t d) -> p t d", t=2)
                                          ).then_inc(acc_free, 1)

                def group(pair, p):
                    g = 2 * pair + p
                    if not (peeled(pair) and g == GROUPS - 1):
                        split_x(g + 1, 1 - p)
                    dve.wait_ge(wst_hi, groups0 + g + 1)
                    cols = bass.ds(GROUP * g, GROUP)
                    low(ws_t[:, 1, :, cols], psum[:, WST_BANK + p, :].rearrange("p (k n) -> p k n", k=KT),
                        ws_t[:, 0, :, cols]).then_inc(wst_lo, 1)
                    if not (peeled(pair) and g == 0):
                        copy_wh(pair + p - 1, 1 - p)
                    dve.wait_ge(wht_hi, groups0 + g + 1)
                    for t in range(2):
                        by_tile = psum[:, WHT_BANK + p, :].rearrange("p (k t n) -> p k t n", k=KT, t=2)
                        last = low(wh_t[:, p, t, 1], by_tile[:, :, t], wh_t[:, p, t, 0])
                    last.then_inc(wht_lo, 1)

                split_x(0, 0)
                each_group(dve, group)
                copy_wh(GROUP_PAIRS - 1, 1)

                def chunk_max(pair, k):
                    n, slot, tile, p, _ = chunk_of(pair, k, 0)
                    dve.wait_ge(scores_done, steps0 + n + 1)
                    nc.vector.tensor_reduce(neg_max[:, slot:slot + 1], psum[:, SCORE_BANK + k % SCORE_BANKS, :],
                                            AXIS_X, ALU.max, negate=True).then_inc(max_done, 1)
                    if k % CHUNKS == CHUNKS - 1:
                        dve.wait_ge(max_done, steps0 + n + 1)
                        nc.vector.tensor_reduce(row_neg_max[:, p:p + 1], neg_max[:, p * CHUNKS:(p + 1) * CHUNKS],
                                                AXIS_X, ALU.min).then_inc(row_max_done, 1)

                def row_weights(pair, k):
                    _, _, tile, p, _ = chunk_of(pair, k, CHUNKS)
                    of, done = slice(p * CHUNKS, (p + 1) * CHUNKS), STAT_STEPS * (tiles0 + tile)
                    dve.wait_ge(factor_done, tiles0 + tile + 1)
                    nc.vector.tensor_tensor(scaled_sum[:, of], factor[:, of], chunk_sum[:, of],
                                            ALU.mult).then_inc(stat_step, 1)
                    dve.wait_ge(stat_step, done + 1)
                    nc.vector.tensor_reduce(row_sum[:, p:p + 1], scaled_sum[:, of], AXIS_X,
                                            ALU.add).then_inc(stat_step, 1)
                    dve.wait_ge(stat_step, done + 2)
                    nc.vector.reciprocal(row_inv[:, p:p + 1], row_sum[:, p:p + 1]).then_inc(stat_step, 1)
                    dve.wait_ge(stat_step, done + 3)
                    nc.vector.tensor_scalar(weight[:, of], factor[:, of], row_inv[:, p:p + 1], None,
                                            ALU.mult).then_inc(stat_step, 1)

                def weigh(pair, k):
                    _, slot, tile, _, _ = chunk_of(pair, k, LAG_WEIGHT)
                    c = slot % CHUNKS
                    piece, column = c // 2, c % 2 * CHUNK
                    if c == 0:
                        dve.wait_ge(stat_step, STAT_STEPS * (tiles0 + tile + 1))
                    if c % 2 == 0:
                        dve.wait_ge(adj_loaded[piece], 16 * (tiles0 + tile + 1))
                    nc.vector.scalar_tensor_tensor(ring[:, slot, :], ring[:, slot, :], weight[:, slot:slot + 1],
                                                   load[:, piece, column:column + CHUNK], ALU.mult,
                                                   ALU.mult).then_inc(a_done, 1)

                def split_a(pair, k):
                    m, slot, _, _, _ = chunk_of(pair, k, LAG_TRANSPOSE)
                    dve.wait_ge(at_hi, steps0 + m + 1)
                    low(moving_lo[:, slot % 2, :], psum[:, AT_BANK + slot % 2, :],
                        moving_hi[:, slot % 2, :]).then_inc(at_lo, 1)

                def finish_rows(pair, k):
                    _, _, tile, p, before = chunk_of(pair, k, LAG_ROWS)
                    acc, y = psum[:, ACC_BANK + p, :], rows[:, p, :]
                    done = sum(ROW_STEPS[:layer]) * TILES + ROW_STEPS[layer] * tile
                    dve.wait_ge(rows_loaded[p], 16 * (layer * PAIRS + before + 1))
                    dve.wait_ge(product_done, steps0 + CHUNKS * (tile + 1))
                    nc.vector.tensor_tensor(y, acc[:, 0:D], y, ALU.add).then_inc(row_step, 1)
                    dve.wait_ge(row_step, done + 1)
                    nc.vector.tensor_tensor(y, acc[:, D:2 * D], y, ALU.add).then_inc(acc_free, 1)
                    dve.wait_ge(acc_free, layer * ACC_FREE + GROUPS + tile + 1)
                    activated = nc.vector.scalar_tensor_tensor(y, y, SLOPE, y, ALU.mult, ALU.max)
                    if not last_layer:
                        activated.then_inc(rows_done, 1)
                        return
                    activated.then_inc(row_step, 1)
                    dve.wait_ge(row_step, done + 2)
                    dve.wait_ge(first_loaded[p], 16 * (before + 1))
                    nc.vector.tensor_tensor(y, y, first_rows[:, p, :], ALU.add).then_inc(row_step, 1)
                    dve.wait_ge(row_step, done + 3)
                    nc.vector.bn_stats(stats[:], y).then_inc(row_step, 1)
                    dve.wait_ge(row_step, done + 4)
                    nc.vector.memset(var_eps[:], EPS)
                    nc.vector.bn_aggr(moments[:], stats[:]).then_inc(row_step, 1)
                    dve.wait_ge(row_step, done + 5)
                    nc.vector.tensor_tensor(var_eps[:], moments[:, 1:2], var_eps[:], ALU.add).then_inc(var_done, 1)

                def normalise_rows(pair, k):
                    _, _, tile, p, _ = chunk_of(pair, k, LAG_NORM)
                    y = rows[:, p, :]
                    dve.wait_ge(inv_std_done, tile + 1)
                    nc.vector.tensor_scalar(y, y, moments[:, 0:1], inv_std[:], ALU.subtract,
                                            ALU.mult).then_inc(rows_done, 1)

                def step(pair, k):
                    if in_stage(pair, k, 0):
                        chunk_max(pair, k)
                    if k % CHUNKS == 0 and in_stage(pair, k, CHUNKS):
                        row_weights(pair, k)
                    if in_stage(pair, k, LAG_WEIGHT):
                        weigh(pair, k)
                    if in_stage(pair, k, LAG_TRANSPOSE):
                        split_a(pair, k)
                    if (k - LAG_ROWS) % CHUNKS == 0 and in_stage(pair, k, LAG_ROWS):
                        finish_rows(pair, k)
                    if last_layer and (k - LAG_NORM) % CHUNKS == 0 and in_stage(pair, k, LAG_NORM):
                        normalise_rows(pair, k)

                each_step(dve, step, LAG_NORM - CHUNKS + 1)

        @block.gpsimd
        def _(pool):
            nc.gpsimd.memset(minus_half[:], -0.5).then_inc(pool_step, 1)
            nc.gpsimd.memset(ident[:], 0.0).then_inc(pool_step, 1)
            pool.wait_ge(pool_step, 2)
            nc.gpsimd.affine_select(out=ident[:], in_=ident[:], compare_op=ALU.not_equal, fill=1.0, base=0,
                                    pattern=[[-1, P]], channel_multiplier=1).then_inc(ident_done, 1)

            for layer in range(LAYERS):
                last_layer = layer == LAYERS - 1

                def load_rows(tile, p):
                    pool.dma_start(rows[:, p, :], in_tiles[layer][tile]).then_inc(rows_loaded[p], 16)
                    if last_layer:
                        pool.dma_start(first_rows[:, p, :], in_tiles[0][tile]).then_inc(first_loaded[p], 16)

                def store_wh_t(pair, p):
                    pool.wait_ge(wht_lo, layer * GROUPS + 2 * pair + p + 1)
                    pool.dma_start(wht_groups[2 * pair + p],
                                   as_f32(wh_t[:, p]).rearrange("p t a k n -> p t (a k n)")
                                   ).then_inc(wht_stored[p], 16)

                def store_rows(tile, p, before):
                    if last_layer:
                        pool.wait_ge(var_done, tile + 1)
                        nc.gpsimd.tensor_tensor(inv_std[:], var_eps[:], minus_half[:],
                                                ALU.pow).then_inc(inv_std_done, 1)
                    pool.wait_ge(rows_done, layer * TILES + tile + 1)
                    pool.dma_start(out_tiles[layer][tile], rows[:, p, :]).then_inc(rows_stored[p], 16)
                    pool.wait_ge(rows_stored[p], 16 * (layer * PAIRS + before + 1))

                load_rows(0, 0)
                load_rows(1, 1)
                for p in range(2):
                    store_wh_t(0, p)
                with pool.Fori(1, GROUP_PAIRS) as pair:
                    for p in range(2):
                        store_wh_t(pair, p)
                with pool.Fori(0, PAIRS - 1) as pair:
                    for p in range(2):
                        store_rows(2 * pair + p, p, pair)
                        load_rows(2 * pair + p + 2, p)
                for p in range(2):
                    store_rows(TILES - 2 + p, p, PAIRS - 1)


def kernel(x, adj, L0_gnn_W_stack):
    import numpy as np
    import concourse.bacc as bacc
    from concourse.bass_utils import run_bass_kernel_spmd

    nc = bacc.Bacc("TRN2", target_bir_lowering=False, num_devices=1)
    arrays = {"x": np.ascontiguousarray(x), "adj": np.ascontiguousarray(adj),
              "w": np.ascontiguousarray(L0_gnn_W_stack)}
    handles = {name: nc.dram_tensor(name, a.shape, mybir.dt.from_np(a.dtype), kind="ExternalInput").ap()
               for name, a in arrays.items()}
    out = nc.dram_tensor("out", arrays["x"].shape, F32, kind="ExternalOutput").ap()
    gat_layernorm(nc, handles["x"], handles["adj"], handles["w"], out)
    return run_bass_kernel_spmd(nc, [arrays], core_ids=[0]).results[0]["out"]
```

```python
from contextlib import ExitStack

import concourse.bass as bass
from concourse import mybir

F32 = mybir.dt.float32
F32R = mybir.dt.float32r
ALU = mybir.AluOpType
ACT = mybir.ActivationFunctionType
AXIS_X = mybir.AxisListType.X

P = 128
LAYERS = 2
SLOPE = 0.01
EPS = 1e-5


def gat_layernorm(nc, x, adj, w, out):
    N, D = x.shape
    KT = D // P
    TILES = N // P
    CHUNK = 512
    CHUNKS = N // CHUNK
    BLOCKS = CHUNK // P
    STEPS = TILES * CHUNKS
    RING = 2 * CHUNKS
    LAG_WEIGHT = CHUNKS + 1
    LAG_TRANSPOSE = CHUNKS + 2
    LAG_SPLIT = CHUNKS + 3
    LAG_PRODUCT = CHUNKS + 4
    LAG_ROWS = CHUNKS + LAG_PRODUCT
    LAG_NORM = LAG_ROWS + 1
    SCORE_BANKS = 4
    ADJ_SLOTS = 4
    PIECE = 2 * CHUNK
    PIECES = N // PIECE
    GROUP = 2 * P
    GROUPS = N // GROUP

    adj_pieces = adj.rearrange("(t p) (q c) -> t q p c", p=P, c=PIECE)
    x1 = nc.dram_tensor("x1_scratch", [N, D], F32).ap()
    qt_tiles = nc.dram_tensor("qt_scratch", [TILES, P, 2 * KT * P], F32).ap()
    qt_groups = qt_tiles.rearrange("(g t) p e -> g p t e", t=2)
    layer_in = [x, x1]
    in_tiles = [a.rearrange("(t p) d -> t p d", p=P) for a in layer_in]
    in_groups = [a.rearrange("(g t p) d -> g p t d", p=P, t=2) for a in layer_in]
    out_tiles = [in_tiles[1], out.rearrange("(t p) d -> t p d", p=P)]

    ctx = ExitStack()
    with ctx:
        def sb(name, shape, dt=F32):
            return ctx.enter_context(nc.sbuf_tensor(name, shape, dt))

        def sem(name):
            return ctx.enter_context(nc.semaphore(name))

        def sem_pair(name):
            return [sem(f"{name}{p}") for p in range(2)]

        x_t = sb("x_t", [P, 2, KT, N], F32R)
        wh = sb("wh", [P, TILES, 2, D], F32R)
        q_t = sb("q_t", [P, 2, 2, 2, KT, P], F32R)
        w_part = sb("w_part", [P, 2, KT, 2 * D], F32R)
        moving_hi = sb("moving_hi", [P, 2, CHUNK], F32R)
        moving_lo = sb("moving_lo", [P, 2, CHUNK], F32R)
        w_t = [[q_t[:, part].rearrange("p t a k n -> p (t a k n)").rearrange("p (b c) -> p b c", b=2)
                for part in range(2)], [moving_hi[:], moving_lo[:]]]
        ring = sb("ring", [P, RING, CHUNK])
        w_rows = ring[:, RING - 4:RING, :].rearrange("p (l k) e -> p l k e", l=LAYERS)
        load = sb("load", [P, ADJ_SLOTS, PIECE])
        rows = sb("rows", [P, 2, D])
        first_rows = sb("first_rows", [P, 2, D])
        ident = sb("ident", [P, P])
        neg_max = sb("neg_max", [P, RING])
        chunk_sum = sb("chunk_sum", [P, RING])
        row_neg_max = sb("row_neg_max", [P, 2])
        factor = sb("factor", [P, RING])
        scaled_sum = sb("scaled_sum", [P, RING])
        row_sum = sb("row_sum", [P, 2])
        row_inv = sb("row_inv", [P, 2])
        weight = sb("weight", [P, RING])
        stats = sb("stats", [P, 6])
        moments = sb("moments", [P, 2])
        var_eps = sb("var_eps", [P, 1])
        minus_half = sb("minus_half", [P, 1])
        inv_std = sb("inv_std", [P, 1])

        psum = ctx.enter_context(nc.psum_tensor("banks", [P, 8, CHUNK], F32))
        XT_BANK, QT_BANK, WT_BANK, WH_BANK = 0, 2, 4, 6
        M_BANK = WT_BANK
        SCORE_BANK, AT_BANK, ACC_BANK = 0, 4, 6

        pool_step, ident_done = sem("pool_step"), sem("ident_done")
        w_loaded = [sem(f"w_loaded{layer}") for layer in range(LAYERS)]
        wt_done, wt_hi, wt_lo = sem("wt_done"), sem("wt_hi"), sem("wt_lo")
        m_done, w_hi, w_lo = sem("m_done"), sem("w_hi"), sem("w_lo")
        x_loaded = sem_pair("x_loaded")
        xt_done, xt_hi, xt_lo = sem("xt_done"), sem("xt_hi"), sem("xt_lo")
        xt_hi_kept, xt_lo_kept = sem("xt_hi_kept"), sem("xt_lo_kept")
        qt_done, qt_hi, qt_lo = sem("qt_done"), sem("qt_hi"), sem("qt_lo")
        wh_done, wh_hi = sem("wh_done"), sem("wh_hi")
        qt_stored, qt_loaded = sem_pair("qt_stored"), sem_pair("qt_loaded")
        adj_loaded = [sem(f"adj_loaded{s}") for s in range(ADJ_SLOTS)]
        scores_done, max_done, exp_done = sem("scores_done"), sem("max_done"), sem("exp_done")
        row_max_done, factor_done = sem("row_max_done"), sem("factor_done")
        stat_step = sem("stat_step")
        a_done, at_done, at_hi, at_lo = sem("a_done"), sem("at_done"), sem("at_hi"), sem("at_lo")
        product_done = sem("product_done")
        acc_free = sem("acc_free")
        row_step = sem("row_step")
        rows_loaded, first_loaded = sem_pair("rows_loaded"), sem_pair("first_loaded")
        var_done, inv_std_done = sem("var_done"), sem("inv_std_done")
        rows_done, rows_stored = sem("rows_done"), sem_pair("rows_stored")

        PAIRS = TILES // 2
        GROUP_PAIRS = GROUPS // 2
        ACC_FREE = GROUPS + TILES
        STAT_STEPS = 4
        STEP_WT, STEP_M = 1, 4
        ROW_STEPS = [1, 5]

        def as_f32(ap):
            return ap.bitcast(F32)

        def peeled(pair):
            return isinstance(pair, int)

        def each_turn(eng, group):
            for p in range(2):
                group(0, p)
            with eng.Fori(1, GROUP_PAIRS - 1) as pair:
                for p in range(2):
                    group(pair, p)
            for p in range(2):
                group(GROUP_PAIRS - 1, p)

        def each_step(eng, step, lag):
            for k in range(RING):
                step(0, k)
            with eng.Fori(1, PAIRS) as pair:
                for k in range(RING):
                    step(pair, k)
            for k in range(lag):
                step(PAIRS, k)

        def in_stage(pair, k, lag):
            return not peeled(pair) or 0 <= RING * pair + k - lag < STEPS

        def chunk_of(pair, k, lag):
            t = (k - lag) // CHUNKS
            return RING * pair + (k - lag), (k - lag) % RING, 2 * pair + t, t % 2, pair + t // 2

        def group_of(pair, p):
            return 0 if peeled(pair) and 2 * pair + p == GROUPS - 1 else 2 * pair + p + 1

        block = ctx.enter_context(nc.Block())

        @block.sync
        def _(sp):
            def load_w(layer):
                sp.dma_start(w_rows[:, layer], w[layer].rearrange("(k p) e -> p k e", p=P)
                             ).then_inc(w_loaded[layer], 16)

            for layer in range(LAYERS):
                groups0, steps0 = layer * GROUPS, layer * STEPS

                def load_x(pair, p):
                    g = group_of(pair, p)
                    if layer:
                        sp.wait_ge(rows_stored[0], 16 * (g + 1))
                        sp.wait_ge(rows_stored[1], 16 * (g + 1))
                    sp.dma_start(load[:, p, 0:2 * D].rearrange("p (t d) -> p t d", t=2),
                                 in_groups[layer][g]).then_inc(x_loaded[p], 16)

                def next_x(pair, p):
                    sp.wait_ge(xt_done, groups0 + 2 * pair + p - 1)
                    load_x(pair, p)

                def store_q_t(pair, p):
                    sp.wait_ge(qt_lo, groups0 + 2 * pair + p + 1)
                    sp.dma_start(qt_groups[group_of(pair, p)],
                                 as_f32(q_t[:, p]).rearrange("p t a k n -> p t (a k n)")
                                 ).then_inc(qt_stored[p], 16)

                if layer:
                    sp.wait_ge(a_done, steps0 - 4)
                else:
                    load_w(0)
                load_x(0, 0)
                load_x(0, 1)
                if not layer:
                    load_w(1)
                next_x(1, 0)
                with sp.Fori(1, GROUP_PAIRS - 1) as pair:
                    next_x(pair, 1)
                    store_q_t(pair - 1, 0)
                    next_x(pair + 1, 0)
                    store_q_t(pair - 1, 1)
                next_x(GROUP_PAIRS - 1, 1)
                store_q_t(GROUP_PAIRS - 2, 0)
                store_q_t(GROUP_PAIRS - 2, 1)
                store_q_t(GROUP_PAIRS - 1, 0)

                def load_q_t(pair, p):
                    sp.dma_start(as_f32(q_t[:, 1, p]).rearrange("p a k n -> p (a k n)"),
                                 qt_tiles[2 * pair + p]).then_inc(qt_loaded[p], 16)

                def load_adj(tile, q):
                    sp.dma_start(load[:, q, :], adj_pieces[tile, q]).then_inc(adj_loaded[q], 16)

                sp.wait_ge(xt_done, groups0 + GROUPS)
                if layer:
                    sp.wait_ge(a_done, steps0)
                for q in range(PIECES):
                    load_adj(0, q)
                sp.wait_ge(qt_stored[0], 16 * GROUP_PAIRS * (layer + 1))
                sp.wait_ge(qt_stored[1], 16 * (GROUP_PAIRS - 1) * (layer + 1))
                with sp.Fori(1, PAIRS) as pair:
                    for p in range(2):
                        sp.wait_ge(scores_done, steps0 + CHUNKS * (2 * pair + p - 1))
                        load_q_t(pair, p)
                        for q in range(PIECES):
                            sp.wait_ge(a_done, steps0 + CHUNKS * (2 * pair + p - 2) + 2 * (q + 1))
                            load_adj(2 * pair + p - 1, q)
                for q in range(PIECES):
                    sp.wait_ge(a_done, steps0 + CHUNKS * (TILES - 2) + 2 * (q + 1))
                    load_adj(TILES - 1, q)

        @block.tensor
        def _(pe):
            def three_products(out_ap, operands):
                for j, (s_hi, s_lo, m_hi, m_lo) in enumerate(operands):
                    nc.tensor.matmul(out_ap, s_hi, m_hi, start=j == 0, stop=False)
                    nc.tensor.matmul(out_ap, s_hi, m_lo, start=False, stop=False)
                    last = nc.tensor.matmul(out_ap, s_lo, m_hi, start=False, stop=j == len(operands) - 1)
                return last

            def transpose_w(layer):
                pe.wait_ge(w_loaded[layer], 16)
                for b in range(2 * KT):
                    for kt in range(KT):
                        last = nc.tensor.transpose(psum[:, WT_BANK + b // 2, (b % 2 * KT + kt) * P:(b % 2 * KT + kt + 1) * P],
                                                   w_rows[:, layer, kt, b * P:(b + 1) * P], ident[:])
                last.then_inc(wt_done, 1)

            def make_m(layer):
                pe.wait_ge(wt_lo, layer + 1)
                for ct in range(KT):
                    last = three_products(
                        psum[:, M_BANK, ct * D:(ct + 1) * D],
                        [(w_t[layer][0][:, 0, et * D + ct * P:et * D + (ct + 1) * P],
                          w_t[layer][1][:, 0, et * D + ct * P:et * D + (ct + 1) * P],
                          w_t[layer][0][:, 1, et * D:(et + 1) * D],
                          w_t[layer][1][:, 1, et * D:(et + 1) * D]) for et in range(KT)])
                last.then_inc(m_done, 1)

            pe.wait_ge(ident_done, 1)
            transpose_w(0)
            for layer in range(LAYERS):
                groups0, steps0 = layer * GROUPS, layer * STEPS

                def transpose_x(p, before):
                    pe.wait_ge(x_loaded[p], 16 * (layer * GROUP_PAIRS + before + 1))
                    for t in range(2):
                        for kt in range(KT):
                            last = nc.tensor.transpose(
                                psum[:, XT_BANK + p, kt * GROUP + t * P:kt * GROUP + (t + 1) * P],
                                load[:, p, t * D + kt * P:t * D + (kt + 1) * P], ident[:])
                    last.then_inc(xt_done, 1)

                def project_q(p):
                    for dt in range(KT):
                        cols = slice(D + dt * P, D + (dt + 1) * P)
                        last = three_products(
                            psum[:, QT_BANK + p, dt * GROUP:(dt + 1) * GROUP],
                            [(w_part[:, 0, kt, cols], w_part[:, 1, kt, cols],
                              moving_hi[:, p, kt * GROUP:(kt + 1) * GROUP],
                              moving_lo[:, p, kt * GROUP:(kt + 1) * GROUP]) for kt in range(KT)])
                    last.then_inc(qt_done, 1)

                def project_wh(p):
                    for t in range(2):
                        of = [slice(kt * GROUP + t * P, kt * GROUP + (t + 1) * P) for kt in range(KT)]
                        last = three_products(
                            psum[:, WH_BANK + p, t * D:(t + 1) * D],
                            [(moving_hi[:, p, of[kt]], moving_lo[:, p, of[kt]],
                              w_part[:, 0, kt, 0:D], w_part[:, 1, kt, 0:D]) for kt in range(KT)])
                    last.then_inc(wh_done, 1)

                def turn(pair, p):
                    n = 2 * pair + p
                    if not (peeled(pair) and n == GROUPS - 1):
                        if not (peeled(pair) and n == 0):
                            pe.wait_ge(xt_lo, groups0 + n)
                        transpose_x(1 - p, pair + p)
                    pe.wait_ge(xt_lo, groups0 + n + 1)
                    if not peeled(pair) or pair > 0:
                        pe.wait_ge(qt_lo, groups0 + n - 1)
                        pe.wait_ge(acc_free, layer * ACC_FREE + n - 1)
                    if peeled(pair) and n == 0:
                        pe.wait_ge(w_lo, 2 * layer + 1)
                        project_wh(p)
                        pe.wait_ge(w_lo, 2 * layer + 2)
                        project_q(p)
                    else:
                        project_q(p)
                        project_wh(p)

                if layer:
                    pe.wait_ge(exp_done, steps0)
                transpose_x(0, 0)
                if layer == 0:
                    make_m(0)
                if layer:
                    pe.wait_ge(acc_free, layer * ACC_FREE)
                each_turn(pe, turn)

                pe.wait_ge(xt_hi_kept, groups0 + GROUPS)
                pe.wait_ge(xt_lo_kept, groups0 + GROUPS)
                pe.wait_ge(qt_lo, groups0 + GROUPS)

                def scores(pair, k):
                    n, slot, _, p, before = chunk_of(pair, k, 0)
                    if k % CHUNKS == 0 and not (peeled(pair) and pair == 0):
                        pe.wait_ge(qt_loaded[p], 16 * (layer * (PAIRS - 1) + before))
                    if not peeled(pair) or n >= SCORE_BANKS:
                        pe.wait_ge(exp_done, steps0 + n - SCORE_BANKS + 1)
                    cols = slice(k % CHUNKS * CHUNK, (k % CHUNKS + 1) * CHUNK)
                    three_products(psum[:, SCORE_BANK + k % SCORE_BANKS, :],
                                   [(q_t[:, 1, p, 0, kt], q_t[:, 1, p, 1, kt],
                                     x_t[:, 0, kt, cols], x_t[:, 1, kt, cols]) for kt in range(KT)]
                                   ).then_inc(scores_done, 1)

                def transpose_a(pair, k):
                    m, slot, _, _, _ = chunk_of(pair, k, LAG_TRANSPOSE)
                    if layer == 0 and peeled(pair) and m == 0:
                        pe.wait_ge(w_lo, 2 * LAYERS)
                    pe.wait_ge(a_done, steps0 + m + 1)
                    if not peeled(pair) or m >= 2:
                        pe.wait_ge(at_lo, steps0 + m - 1)
                    for b in range(BLOCKS):
                        last = nc.tensor.transpose(psum[:, AT_BANK + slot % 2, b * P:(b + 1) * P],
                                                   ring[:, slot, b * P:(b + 1) * P], ident[:])
                    last.then_inc(at_done, 1)

                def product(pair, k):
                    m, slot, tile, p, _ = chunk_of(pair, k, LAG_PRODUCT)
                    bank, c = ACC_BANK + p, slot % CHUNKS
                    pe.wait_ge(at_lo, steps0 + m + 1)
                    if c == 0:
                        free = 0 if peeled(pair) and tile < 2 else tile - 1
                        pe.wait_ge(acc_free, layer * ACC_FREE + GROUPS + free)
                    for b in range(BLOCKS):
                        j, of = c * BLOCKS + b, slice(b * P, (b + 1) * P)
                        start, stop = j == 0, j == TILES - 1
                        nc.tensor.matmul(psum[:, bank, :], moving_hi[:, slot % 2, of],
                                         wh[:, j].rearrange("p a d -> p (a d)"),
                                         start=start, stop=stop, skip_group_check=True)
                        last = nc.tensor.matmul(psum[:, bank, 0:D], moving_lo[:, slot % 2, of], wh[:, j, 0],
                                                start=False, stop=stop, skip_group_check=True)
                    last.then_inc(product_done, 1)

                def step(pair, k):
                    if in_stage(pair, k, 0):
                        scores(pair, k)
                    if layer == 0 and peeled(pair) and pair == 0:
                        if k == STEP_WT:
                            transpose_w(1)
                        if k == STEP_M:
                            make_m(1)
                    if in_stage(pair, k, LAG_TRANSPOSE):
                        transpose_a(pair, k)
                    if in_stage(pair, k, LAG_PRODUCT):
                        product(pair, k)

                each_step(pe, step, LAG_PRODUCT)

        @block.scalar
        def _(act):
            def split_wt(layer):
                act.wait_ge(wt_done, layer + 1)
                nc.scalar.activation(w_t[layer][0], psum[:, WT_BANK:WT_BANK + 2, :], ACT.Copy).then_inc(wt_hi, 1)

            def split_w(layer):
                act.wait_ge(w_loaded[layer], 16)
                nc.scalar.activation(w_part[:, 0, :, 0:D], w_rows[:, layer, :, 0:D], ACT.Copy).then_inc(w_hi, 1)
                act.wait_ge(m_done, layer + 1)
                nc.scalar.activation(w_part[:, 0, :, D:2 * D],
                                     psum[:, M_BANK, :].rearrange("p (k e) -> p k e", k=KT),
                                     ACT.Copy).then_inc(w_hi, 1)

            split_wt(0)
            for layer in range(LAYERS):
                groups0, steps0, tiles0 = layer * GROUPS, layer * STEPS, layer * TILES

                def split_x(n, p, free):
                    act.wait_ge(xt_done, groups0 + n + 1)
                    if not free:
                        act.wait_ge(wh_done, groups0 + n - 1)
                        act.wait_ge(xt_hi_kept, groups0 + n - 1)
                    nc.scalar.activation(moving_hi[:, p, :], psum[:, XT_BANK + p, :], ACT.Copy).then_inc(xt_hi, 1)

                def turn(pair, p):
                    n, g = 2 * pair + p, group_of(pair, p)
                    if not (peeled(pair) and n == GROUPS - 1):
                        split_x(n + 1, 1 - p, peeled(pair) and n == 0)
                    act.wait_ge(xt_hi, groups0 + n + 1)
                    nc.scalar.activation(x_t[:, 0, :, bass.ds(GROUP * g, GROUP)],
                                         as_f32(moving_hi[:, p, :]).rearrange("p (k n) -> p k n", k=KT),
                                         ACT.Copy).then_inc(xt_hi_kept, 1)
                    act.wait_ge(qt_done, groups0 + n + 1)
                    if not peeled(pair) or pair > 0:
                        act.wait_ge(qt_stored[p], 16 * (layer * (GROUP_PAIRS - p) + pair))
                    for t in range(2):
                        by_tile = psum[:, QT_BANK + p, :].rearrange("p (k t n) -> p k t n", k=KT, t=2)
                        last = nc.scalar.activation(q_t[:, p, t, 0], by_tile[:, :, t], ACT.Copy)
                    last.then_inc(qt_hi, 1)
                    act.wait_ge(wh_done, groups0 + n + 1)
                    nc.scalar.activation(wh[:, bass.ds(2 * g, 2), 0, :],
                                         psum[:, WH_BANK + p, :].rearrange("p (t d) -> p t d", t=2),
                                         ACT.Copy).then_inc(wh_hi, 1)

                split_x(0, 0, True)
                if layer == 0:
                    split_w(0)
                each_turn(act, turn)

                def exponentials(pair, k):
                    n, slot, tile, p, _ = chunk_of(pair, k, 0)
                    act.wait_ge(max_done, steps0 + n + 1)
                    if layer == 0 and peeled(pair) and n == RING - 4:
                        act.wait_ge(w_lo, 2 * LAYERS)
                    if not peeled(pair):
                        act.wait_ge(at_done, steps0 + n - RING + 1)
                    nc.scalar.activation(ring[:, slot, :], psum[:, SCORE_BANK + k % SCORE_BANKS, :], ACT.Exp,
                                         bias=neg_max[:, slot:slot + 1],
                                         accum_out=chunk_sum[:, slot:slot + 1]).then_inc(exp_done, 1)
                    if k % CHUNKS == CHUNKS - 1:
                        of = slice(p * CHUNKS, (p + 1) * CHUNKS)
                        act.wait_ge(row_max_done, tiles0 + tile + 1)
                        nc.scalar.activation(factor[:, of], neg_max[:, of], ACT.Exp,
                                             bias=row_neg_max[:, p:p + 1], scale=-1.0).then_inc(factor_done, 1)

                def split_a(pair, k):
                    m, slot, _, _, _ = chunk_of(pair, k, LAG_SPLIT)
                    act.wait_ge(at_done, steps0 + m + 1)
                    if not peeled(pair) or m >= 2:
                        act.wait_ge(product_done, steps0 + m - 1)
                    nc.scalar.activation(moving_hi[:, slot % 2, :], psum[:, AT_BANK + slot % 2, :],
                                         ACT.Copy).then_inc(at_hi, 1)

                def step(pair, k):
                    if layer == 0 and peeled(pair) and pair == 0:
                        if k == STEP_WT + 1:
                            split_wt(1)
                        if k == STEP_M + 1:
                            split_w(1)
                    if in_stage(pair, k, LAG_SPLIT):
                        split_a(pair, k)
                    if in_stage(pair, k, 0):
                        exponentials(pair, k)

                each_step(act, step, LAG_SPLIT)

        @block.vector
        def _(dve):
            def low(out_ap, value, hi):
                return nc.vector.tensor_tensor(out_ap, value, as_f32(hi), ALU.subtract)

            def split_wt(layer):
                dve.wait_ge(wt_hi, layer + 1)
                low(w_t[layer][1], psum[:, WT_BANK:WT_BANK + 2, :], w_t[layer][0]).then_inc(wt_lo, 1)

            def split_w(layer):
                dve.wait_ge(w_hi, 2 * layer + 1)
                low(w_part[:, 1, :, 0:D], w_rows[:, layer, :, 0:D], w_part[:, 0, :, 0:D]).then_inc(w_lo, 1)
                dve.wait_ge(w_hi, 2 * layer + 2)
                low(w_part[:, 1, :, D:2 * D], psum[:, M_BANK, :].rearrange("p (k e) -> p k e", k=KT),
                    w_part[:, 0, :, D:2 * D]).then_inc(w_lo, 1)

            split_wt(0)
            for layer in range(LAYERS):
                groups0, steps0, tiles0 = layer * GROUPS, layer * STEPS, layer * TILES
                last_layer = layer == LAYERS - 1

                def split_x(n, p, free):
                    if not free:
                        dve.wait_ge(xt_lo_kept, groups0 + n - 1)
                    dve.wait_ge(xt_hi, groups0 + n + 1)
                    low(moving_lo[:, p, :], psum[:, XT_BANK + p, :], moving_hi[:, p, :]).then_inc(xt_lo, 1)

                def turn(pair, p):
                    n, g = 2 * pair + p, group_of(pair, p)
                    if not (peeled(pair) and n == GROUPS - 1):
                        split_x(n + 1, 1 - p, peeled(pair) and n == 0)
                    dve.wait_ge(xt_lo, groups0 + n + 1)
                    nc.vector.tensor_copy(x_t[:, 1, :, bass.ds(GROUP * g, GROUP)],
                                          as_f32(moving_lo[:, p, :]).rearrange("p (k n) -> p k n", k=KT)
                                          ).then_inc(xt_lo_kept, 1)
                    dve.wait_ge(qt_hi, groups0 + n + 1)
                    for t in range(2):
                        by_tile = psum[:, QT_BANK + p, :].rearrange("p (k t n) -> p k t n", k=KT, t=2)
                        last = low(q_t[:, p, t, 1], by_tile[:, :, t], q_t[:, p, t, 0])
                    last.then_inc(qt_lo, 1)
                    dve.wait_ge(wh_hi, groups0 + n + 1)
                    tiles = bass.ds(2 * g, 2)
                    low(wh[:, tiles, 1, :], psum[:, WH_BANK + p, :].rearrange("p (t d) -> p t d", t=2),
                        wh[:, tiles, 0, :]).then_inc(acc_free, 1)

                split_x(0, 0, True)
                if layer == 0:
                    split_w(0)
                each_turn(dve, turn)

                def chunk_max(pair, k):
                    n, slot, tile, p, _ = chunk_of(pair, k, 0)
                    dve.wait_ge(scores_done, steps0 + n + 1)
                    nc.vector.tensor_reduce(neg_max[:, slot:slot + 1], psum[:, SCORE_BANK + k % SCORE_BANKS, :],
                                            AXIS_X, ALU.max, negate=True).then_inc(max_done, 1)
                    if k % CHUNKS == CHUNKS - 1:
                        dve.wait_ge(max_done, steps0 + n + 1)
                        nc.vector.tensor_reduce(row_neg_max[:, p:p + 1], neg_max[:, p * CHUNKS:(p + 1) * CHUNKS],
                                                AXIS_X, ALU.min).then_inc(row_max_done, 1)

                def row_weights(pair, k):
                    _, _, tile, p, _ = chunk_of(pair, k, CHUNKS)
                    of, done = slice(p * CHUNKS, (p + 1) * CHUNKS), STAT_STEPS * (tiles0 + tile)
                    dve.wait_ge(factor_done, tiles0 + tile + 1)
                    nc.vector.tensor_tensor(scaled_sum[:, of], factor[:, of], chunk_sum[:, of],
                                            ALU.mult).then_inc(stat_step, 1)
                    dve.wait_ge(stat_step, done + 1)
                    nc.vector.tensor_reduce(row_sum[:, p:p + 1], scaled_sum[:, of], AXIS_X,
                                            ALU.add).then_inc(stat_step, 1)
                    dve.wait_ge(stat_step, done + 2)
                    nc.vector.reciprocal(row_inv[:, p:p + 1], row_sum[:, p:p + 1]).then_inc(stat_step, 1)
                    dve.wait_ge(stat_step, done + 3)
                    nc.vector.tensor_scalar(weight[:, of], factor[:, of], row_inv[:, p:p + 1], None,
                                            ALU.mult).then_inc(stat_step, 1)

                def weigh(pair, k):
                    _, slot, tile, _, _ = chunk_of(pair, k, LAG_WEIGHT)
                    c = slot % CHUNKS
                    piece, column = c // 2, c % 2 * CHUNK
                    if c == 0:
                        dve.wait_ge(stat_step, STAT_STEPS * (tiles0 + tile + 1))
                    if c % 2 == 0:
                        dve.wait_ge(adj_loaded[piece], 16 * (tiles0 + tile + 1))
                    nc.vector.scalar_tensor_tensor(ring[:, slot, :], ring[:, slot, :], weight[:, slot:slot + 1],
                                                   load[:, piece, column:column + CHUNK], ALU.mult,
                                                   ALU.mult).then_inc(a_done, 1)

                def split_a(pair, k):
                    m, slot, _, _, _ = chunk_of(pair, k, LAG_SPLIT)
                    dve.wait_ge(at_hi, steps0 + m + 1)
                    low(moving_lo[:, slot % 2, :], psum[:, AT_BANK + slot % 2, :],
                        moving_hi[:, slot % 2, :]).then_inc(at_lo, 1)

                def finish_rows(pair, k):
                    _, _, tile, p, before = chunk_of(pair, k, LAG_ROWS)
                    acc, y = psum[:, ACC_BANK + p, :], rows[:, p, :]
                    done = sum(ROW_STEPS[:layer]) * TILES + ROW_STEPS[layer] * tile
                    dve.wait_ge(rows_loaded[p], 16 * (layer * PAIRS + before + 1))
                    dve.wait_ge(product_done, steps0 + CHUNKS * (tile + 1))
                    nc.vector.tensor_tensor(y, acc[:, 0:D], y, ALU.add).then_inc(row_step, 1)
                    dve.wait_ge(row_step, done + 1)
                    nc.vector.tensor_tensor(y, acc[:, D:2 * D], y, ALU.add).then_inc(acc_free, 1)
                    dve.wait_ge(acc_free, layer * ACC_FREE + GROUPS + tile + 1)
                    activated = nc.vector.scalar_tensor_tensor(y, y, SLOPE, y, ALU.mult, ALU.max)
                    if not last_layer:
                        activated.then_inc(rows_done, 1)
                        return
                    activated.then_inc(row_step, 1)
                    dve.wait_ge(row_step, done + 2)
                    dve.wait_ge(first_loaded[p], 16 * (before + 1))
                    nc.vector.tensor_tensor(y, y, first_rows[:, p, :], ALU.add).then_inc(row_step, 1)
                    dve.wait_ge(row_step, done + 3)
                    nc.vector.bn_stats(stats[:], y).then_inc(row_step, 1)
                    dve.wait_ge(row_step, done + 4)
                    nc.vector.memset(var_eps[:], EPS)
                    nc.vector.bn_aggr(moments[:], stats[:]).then_inc(row_step, 1)
                    dve.wait_ge(row_step, done + 5)
                    nc.vector.tensor_tensor(var_eps[:], moments[:, 1:2], var_eps[:], ALU.add).then_inc(var_done, 1)

                def normalise_rows(pair, k):
                    _, _, tile, p, _ = chunk_of(pair, k, LAG_NORM)
                    y = rows[:, p, :]
                    dve.wait_ge(inv_std_done, tile + 1)
                    nc.vector.tensor_scalar(y, y, moments[:, 0:1], inv_std[:], ALU.subtract,
                                            ALU.mult).then_inc(rows_done, 1)

                def step(pair, k):
                    if layer == 0 and peeled(pair) and pair == 0:
                        if k == STEP_WT + 1:
                            split_wt(1)
                        if k == STEP_M + 1:
                            split_w(1)
                    if in_stage(pair, k, LAG_WEIGHT):
                        weigh(pair, k)
                    if in_stage(pair, k, LAG_SPLIT):
                        split_a(pair, k)
                    if in_stage(pair, k, 0):
                        chunk_max(pair, k)
                    if k % CHUNKS == 0 and in_stage(pair, k, CHUNKS):
                        row_weights(pair, k)
                    if (k - LAG_ROWS) % CHUNKS == 0 and in_stage(pair, k, LAG_ROWS):
                        finish_rows(pair, k)
                    if last_layer and (k - LAG_NORM) % CHUNKS == 0 and in_stage(pair, k, LAG_NORM):
                        normalise_rows(pair, k)

                each_step(dve, step, LAG_NORM - CHUNKS + 1)

        @block.gpsimd
        def _(pool):
            nc.gpsimd.memset(minus_half[:], -0.5).then_inc(pool_step, 1)
            nc.gpsimd.memset(ident[:], 0.0).then_inc(pool_step, 1)
            pool.wait_ge(pool_step, 2)
            nc.gpsimd.affine_select(out=ident[:], in_=ident[:], compare_op=ALU.not_equal, fill=1.0, base=0,
                                    pattern=[[-1, P]], channel_multiplier=1).then_inc(ident_done, 1)

            for layer in range(LAYERS):
                last_layer = layer == LAYERS - 1

                def load_rows(tile, p):
                    pool.dma_start(rows[:, p, :], in_tiles[layer][tile]).then_inc(rows_loaded[p], 16)
                    if last_layer:
                        pool.dma_start(first_rows[:, p, :], in_tiles[0][tile]).then_inc(first_loaded[p], 16)

                def store_rows(tile, p, before):
                    if last_layer:
                        pool.wait_ge(var_done, tile + 1)
                        nc.gpsimd.tensor_tensor(inv_std[:], var_eps[:], minus_half[:],
                                                ALU.pow).then_inc(inv_std_done, 1)
                    pool.wait_ge(rows_done, layer * TILES + tile + 1)
                    pool.dma_start(out_tiles[layer][tile], rows[:, p, :]).then_inc(rows_stored[p], 16)
                    pool.wait_ge(rows_stored[p], 16 * (layer * PAIRS + before + 1))

                load_rows(0, 0)
                load_rows(1, 1)
                with pool.Fori(0, PAIRS - 1) as pair:
                    for p in range(2):
                        store_rows(2 * pair + p, p, pair)
                        load_rows(2 * pair + p + 2, p)
                for p in range(2):
                    store_rows(TILES - 2 + p, p, PAIRS - 1)


def kernel(x, adj, L0_gnn_W_stack):
    import numpy as np
    import concourse.bacc as bacc
    from concourse.bass_utils import run_bass_kernel_spmd

    nc = bacc.Bacc("TRN2", target_bir_lowering=False, num_devices=1)
    arrays = {"x": np.ascontiguousarray(x), "adj": np.ascontiguousarray(adj),
              "w": np.ascontiguousarray(L0_gnn_W_stack)}
    handles = {name: nc.dram_tensor(name, a.shape, mybir.dt.from_np(a.dtype), kind="ExternalInput").ap()
               for name, a in arrays.items()}
    out = nc.dram_tensor("out", arrays["x"].shape, F32, kind="ExternalOutput").ap()
    gat_layernorm(nc, handles["x"], handles["adj"], handles["w"], out)
    return run_bass_kernel_spmd(nc, [arrays], core_ids=[0]).results[0]["out"]
```
